# Optimizing a Trainium2 kernel written in Bass

```python
import numpy as np
import jax
import jax.numpy as jnp

def _softmax(x, axis=-1):
    return jax.nn.softmax(x, axis=axis)

def _gelu(x):
    return jax.nn.gelu(x, approximate=True)

def _silu(x):
    return jax.nn.silu(x)

def _sigmoid(x):
    return jax.nn.sigmoid(x)

def _layernorm(x, axis=-1, eps=1e-05):
    m = jnp.mean(x, axis=axis, keepdims=True)
    v = jnp.var(x, axis=axis, keepdims=True)
    return (x - m) / jnp.sqrt(v + eps)

def _scatter_add(tgt, idx, src, axis=0):
    return tgt.at[idx].add(src)

def _segment_sum(src, seg, n):
    return jax.ops.segment_sum(src, seg, n)
kernel_name = 'mk_dlrm_tower_d1_rec_r8_af24ac'

def setup_inputs(seed: int=0):
    np.random.seed(seed)
    _w = jnp.asarray

    def _rec_inputs():
        import jax
        import jax.numpy as jnp
        _tk = jax.random.key(seed)
        ids = jnp.stack([jax.random.randint(jax.random.fold_in(_tk, 200 + f), (512,), 0, v, jnp.int32) for f, v in enumerate([1250, 12500, 12500, 1250, 1250, 125000, 12500, 12500, 1000, 12500, 1250, 1000, 1250, 1250, 1000, 1000, 1000, 12500, 1250, 12500, 12500, 1000, 1000, 1000, 1250, 1000])], axis=1)
        tbl_0 = 0.05 * jax.random.normal(jax.random.fold_in(_tk, 500 + 0), (1250, 128), jnp.float32)
        tbl_1 = 0.05 * jax.random.normal(jax.random.fold_in(_tk, 500 + 1), (12500, 128), jnp.float32)
        tbl_2 = 0.05 * jax.random.normal(jax.random.fold_in(_tk, 500 + 2), (12500, 128), jnp.float32)
        tbl_3 = 0.05 * jax.random.normal(jax.random.fold_in(_tk, 500 + 3), (1250, 128), jnp.float32)
        tbl_4 = 0.05 * jax.random.normal(jax.random.fold_in(_tk, 500 + 4), (1250, 128), jnp.float32)
        tbl_5 = 0.05 * jax.random.normal(jax.random.fold_in(_tk, 500 + 5), (125000, 128), jnp.float32)
        tbl_6 = 0.05 * jax.random.normal(jax.random.fold_in(_tk, 500 + 6), (12500, 128), jnp.float32)
        tbl_7 = 0.05 * jax.random.normal(jax.random.fold_in(_tk, 500 + 7), (12500, 128), jnp.float32)
        tbl_8 = 0.05 * jax.random.normal(jax.random.fold_in(_tk, 500 + 8), (1000, 128), jnp.float32)
        tbl_9 = 0.05 * jax.random.normal(jax.random.fold_in(_tk, 500 + 9), (12500, 128), jnp.float32)
        tbl_10 = 0.05 * jax.random.normal(jax.random.fold_in(_tk, 500 + 10), (1250, 128), jnp.float32)
        tbl_11 = 0.05 * jax.random.normal(jax.random.fold_in(_tk, 500 + 11), (1000, 128), jnp.float32)
        tbl_12 = 0.05 * jax.random.normal(jax.random.fold_in(_tk, 500 + 12), (1250, 128), jnp.float32)
        tbl_13 = 0.05 * jax.random.normal(jax.random.fold_in(_tk, 500 + 13), (1250, 128), jnp.float32)
        tbl_14 = 0.05 * jax.random.normal(jax.random.fold_in(_tk, 500 + 14), (1000, 128), jnp.float32)
        tbl_15 = 0.05 * jax.random.normal(jax.random.fold_in(_tk, 500 + 15), (1000, 128), jnp.float32)
        tbl_16 = 0.05 * jax.random.normal(jax.random.fold_in(_tk, 500 + 16), (1000, 128), jnp.float32)
        tbl_17 = 0.05 * jax.random.normal(jax.random.fold_in(_tk, 500 + 17), (12500, 128), jnp.float32)
        tbl_18 = 0.05 * jax.random.normal(jax.random.fold_in(_tk, 500 + 18), (1250, 128), jnp.float32)
        tbl_19 = 0.05 * jax.random.normal(jax.random.fold_in(_tk, 500 + 19), (12500, 128), jnp.float32)
        tbl_20 = 0.05 * jax.random.normal(jax.random.fold_in(_tk, 500 + 20), (12500, 128), jnp.float32)
        tbl_21 = 0.05 * jax.random.normal(jax.random.fold_in(_tk, 500 + 21), (1000, 128), jnp.float32)
        tbl_22 = 0.05 * jax.random.normal(jax.random.fold_in(_tk, 500 + 22), (1000, 128), jnp.float32)
        tbl_23 = 0.05 * jax.random.normal(jax.random.fold_in(_tk, 500 + 23), (1000, 128), jnp.float32)
        tbl_24 = 0.05 * jax.random.normal(jax.random.fold_in(_tk, 500 + 24), (1250, 128), jnp.float32)
        tbl_25 = 0.05 * jax.random.normal(jax.random.fold_in(_tk, 500 + 25), (1000, 128), jnp.float32)
        _rk = jax.random.fold_in(_tk, 7)
        r_dense_features = -0.000520686 + 1.00062 * jax.random.normal(jax.random.fold_in(_rk, 101), (512, 128), jnp.float32)
        W_top1 = 0.0405887 * jax.random.normal(jax.random.fold_in(_tk, 801), (607, 512), jnp.float32)
        W_top2 = 0.0441942 * jax.random.normal(jax.random.fold_in(_tk, 802), (512, 256), jnp.float32)
        W_top3 = 0.0625 * jax.random.normal(jax.random.fold_in(_tk, 803), (256, 1), jnp.float32)
        b_top1 = jnp.zeros((512,), jnp.float32)
        b_top2 = jnp.zeros((256,), jnp.float32)
        return (r_dense_features, ids, tbl_0, tbl_1, tbl_2, tbl_3, tbl_4, tbl_5, tbl_6, tbl_7, tbl_8, tbl_9, tbl_10, tbl_11, tbl_12, tbl_13, tbl_14, tbl_15, tbl_16, tbl_17, tbl_18, tbl_19, tbl_20, tbl_21, tbl_22, tbl_23, tbl_24, tbl_25, W_top1, b_top1, W_top2, b_top2, W_top3)
    r_dense_features, ids, tbl_0, tbl_1, tbl_2, tbl_3, tbl_4, tbl_5, tbl_6, tbl_7, tbl_8, tbl_9, tbl_10, tbl_11, tbl_12, tbl_13, tbl_14, tbl_15, tbl_16, tbl_17, tbl_18, tbl_19, tbl_20, tbl_21, tbl_22, tbl_23, tbl_24, tbl_25, W_top1, b_top1, W_top2, b_top2, W_top3 = _rec_inputs()

    def _L0_rec_setup():
        import jax, jax.numpy as jnp
        import numpy as np
        F = 26
        N = F + 1
        _TRIU_I, _TRIU_J = np.triu_indices(N, k=1)
        key = jax.random.key(seed)
        k1, k2 = jax.random.split(key)
        B, D = (2048, 128)
        dense_features = jax.random.normal(k1, (B, D), dtype=jnp.float32)
        sparse_features = jax.random.normal(k2, (B, F, D), dtype=jnp.float32)
        return {'dense_features': dense_features, 'sparse_features': sparse_features}
    _L0_rec_all = _L0_rec_setup()
    _L0_rec_in = {k: v for k, v in _L0_rec_all.items() if k in ()}
    del _L0_rec_all
    return {'r_dense_features': r_dense_features, 'ids': ids, 'tbl_0': tbl_0, 'tbl_1': tbl_1, 'tbl_2': tbl_2, 'tbl_3': tbl_3, 'tbl_4': tbl_4, 'tbl_5': tbl_5, 'tbl_6': tbl_6, 'tbl_7': tbl_7, 'tbl_8': tbl_8, 'tbl_9': tbl_9, 'tbl_10': tbl_10, 'tbl_11': tbl_11, 'tbl_12': tbl_12, 'tbl_13': tbl_13, 'tbl_14': tbl_14, 'tbl_15': tbl_15, 'tbl_16': tbl_16, 'tbl_17': tbl_17, 'tbl_18': tbl_18, 'tbl_19': tbl_19, 'tbl_20': tbl_20, 'tbl_21': tbl_21, 'tbl_22': tbl_22, 'tbl_23': tbl_23, 'tbl_24': tbl_24, 'tbl_25': tbl_25, 'W_top1': W_top1, 'b_top1': b_top1, 'W_top2': W_top2, 'b_top2': b_top2, 'W_top3': W_top3}

def reference(r_dense_features, ids, tbl_0, tbl_1, tbl_2, tbl_3, tbl_4, tbl_5, tbl_6, tbl_7, tbl_8, tbl_9, tbl_10, tbl_11, tbl_12, tbl_13, tbl_14, tbl_15, tbl_16, tbl_17, tbl_18, tbl_19, tbl_20, tbl_21, tbl_22, tbl_23, tbl_24, tbl_25, W_top1, b_top1, W_top2, b_top2, W_top3):
    import jax
    import jax.numpy as jnp

    def _L0_rec_ref(dense_features, sparse_features):
        import jax, jax.numpy as jnp
        import numpy as np
        F = 26
        N = F + 1
        _TRIU_I, _TRIU_J = np.triu_indices(N, k=1)
        combined = jnp.concatenate([dense_features[:, None, :], sparse_features], axis=1)
        interactions = jnp.einsum('bnd,bmd->bnm', combined, combined)
        interactions_flat = interactions[:, _TRIU_I, _TRIU_J]
        return jnp.concatenate([dense_features, interactions_flat], axis=1)
    e = jnp.stack([tbl_0[ids[:, 0]], tbl_1[ids[:, 1]], tbl_2[ids[:, 2]], tbl_3[ids[:, 3]], tbl_4[ids[:, 4]], tbl_5[ids[:, 5]], tbl_6[ids[:, 6]], tbl_7[ids[:, 7]], tbl_8[ids[:, 8]], tbl_9[ids[:, 9]], tbl_10[ids[:, 10]], tbl_11[ids[:, 11]], tbl_12[ids[:, 12]], tbl_13[ids[:, 13]], tbl_14[ids[:, 14]], tbl_15[ids[:, 15]], tbl_16[ids[:, 16]], tbl_17[ids[:, 17]], tbl_18[ids[:, 18]], tbl_19[ids[:, 19]], tbl_20[ids[:, 20]], tbl_21[ids[:, 21]], tbl_22[ids[:, 22]], tbl_23[ids[:, 23]], tbl_24[ids[:, 24]], tbl_25[ids[:, 25]]], axis=1)
    z = _L0_rec_ref(r_dense_features, e)
    z = z.reshape(z.shape[0], -1)
    h = jnp.concatenate([z, r_dense_features], axis=1)
    h = jnp.maximum(h @ W_top1 + b_top1, 0.0)
    h = jnp.maximum(h @ W_top2 + b_top2, 0.0)
    y = h @ W_top3
    return y

_drawn_inputs = setup_inputs


def setup_inputs(seed=0):
    import zlib

    import numpy as np

    out = dict(_drawn_inputs(seed))
    spreads = {'b_top1': (0.0, 0.1), 'b_top2': (0.0, 0.1)}
    factors = {}
    for name, (base, spread) in spreads.items():
        noise = np.random.default_rng([zlib.crc32(name.encode()), seed]).standard_normal(out[name].shape)
        drawn = base * np.exp(spread * noise) if base else spread * noise
        out[name] = jnp.asarray(drawn.astype(out[name].dtype))
    for name, factor in factors.items():
        out[name] = (out[name] * factor).astype(out[name].dtype)
    return out
```

```python
from contextlib import ExitStack

import numpy as np

import concourse.bass as bass
from concourse import mybir

P = 128
TABLES = 26
SLOTS = TABLES + 1
SIDE = SLOTS - 1
QUAD = 32
PER_BANK = 4
KEPT = [(0, 4, 4), (4, 8, 8), (8, 12, 12), (12, 16, 16), (16, 20, 20),
        (20, 22, 22), (22, 24, 24), (24, 25, 26), (25, 26, 26)]
KEPT_BY_VECTOR = 5
KEPT_AT = np.cumsum([0] + [(stop - start) * width for start, stop, width in KEPT]).tolist()
PAIR_BLOCKS = KEPT_AT[-1] // P
assert KEPT_AT[-1] == PAIR_BLOCKS * P

F32 = mybir.dt.float32
I32 = mybir.dt.int32
ALU = mybir.AluOpType
ACT = mybir.ActivationFunctionType


def dlrm_tower(nc, dense, ids, tables, identity, w_pairs, w_dense, b1, w2, b2, w3, y):
    batch = dense.shape[0]
    hidden1, hidden2 = w_pairs.shape[2], w2.shape[2]
    TILES = batch // P
    UNITS1 = hidden1 // P
    UNITS2 = hidden2 // P
    H1_HALF = UNITS1 // 2
    GROUPS = -(-SLOTS // PER_BANK)

    def slots_of(g):
        return range(g * PER_BANK, min(SLOTS, (g + 1) * PER_BANK))

    with ExitStack() as ctx:
        def sb(name, shape, dt=F32):
            return ctx.enter_context(nc.sbuf_tensor(name, shape, dt))

        def psum(name, shape):
            return ctx.enter_context(nc.psum_tensor(name, shape, F32))

        def sem(name):
            return ctx.enter_context(nc.semaphore(name))

        ids_sb = sb("ids_sb", [P, TILES * TABLES], I32)
        rows = sb("rows", [P, TILES, SLOTS, P])
        eye = sb("eye", [P, P])
        features = sb("features", [P, batch, SLOTS])
        products = sb("products", [P, SIDE, QUAD])
        kept = sb("kept", [P, 2, PAIR_BLOCKS * P])
        pairs = sb("pairs", [P, 2, PAIR_BLOCKS, P])
        w_pairs_sb = sb("w_pairs_sb", [P, PAIR_BLOCKS, hidden1])
        w_dense_sb = sb("w_dense_sb", [P, 2, hidden1])
        w_dense_sum = sb("w_dense_sum", [P, hidden1])
        b1_sb = sb("b1_sb", [P, UNITS1])
        w2_sb = sb("w2_sb", [P, UNITS1, hidden2])
        b2_sb = sb("b2_sb", [P, UNITS2])
        w3_sb = sb("w3_sb", [P, UNITS2])
        h1 = sb("h1", [P, UNITS1, P])
        h2 = sb("h2", [P, UNITS2, P])
        y_sb = sb("y_sb", [1, batch])

        turned_ps = [psum(f"turned_ps{i}", [P, PER_BANK, P]) for i in range(2)]
        gram_ps = psum("gram_ps", [P, QUAD, QUAD])
        pairs_ps = psum("pairs_ps", [P, PAIR_BLOCKS, P])
        h1_ps = [psum(f"h1_ps{i}", [P, UNITS1 // 2, P]) for i in range(2)]
        h2_y_ps = psum("h2_y_ps", [P, UNITS2 + 1, P])
        h2_ps = h2_y_ps[:, 0:UNITS2, :]
        y_ps = h2_y_ps[0:1, UNITS2, :]

        ids_in = sem("ids_in")
        eye_in = sem("eye_in")
        dense_in = sem("dense_in")
        w1_in = sem("w1_in")
        w_rest_in = sem("w_rest_in")
        gathered = [[sem(f"gathered_{t}_{g}") for g in range(GROUPS)] for t in range(TILES)]
        gram_cleared = sem("gram_cleared")
        w_dense_summed = sem("w_dense_summed")
        turned = sem("turned")
        features_act = sem("features_act")
        features_dve = sem("features_dve")
        gram_done = sem("gram_done")
        products_done = sem("products_done")
        kept_dve = sem("kept_dve")
        kept_act = sem("kept_act")
        pairs_turned = sem("pairs_turned")
        pairs_copied = sem("pairs_copied")
        h1_done = sem("h1_done")
        h1_relu_act = sem("h1_relu_act")
        h1_relu_dve = sem("h1_relu_dve")
        h2_done = sem("h2_done")
        h2_relu = sem("h2_relu")
        y_done = sem("y_done")
        y_copied = sem("y_copied")
        y_out = sem("y_out")

        block = ctx.enter_context(nc.Block())

        @block.sync
        def _(sp):
            sp.dma_start(ids_sb[:, :], ids).then_inc(ids_in, 16)
            sp.dma_start(eye[:, :], identity).then_inc(eye_in, 16)
            sp.dma_start(rows[:, :, 0, :], dense.rearrange("(t p) d -> p t d", p=P)).then_inc(dense_in, 16)
            sp.dma_start(w_dense_sb[:, :, :], w_dense).then_inc(w1_in, 16)
            sp.dma_start(w_pairs_sb[:, :, :], w_pairs).then_inc(w1_in, 16)
            sp.dma_start(b1_sb[:, :], b1).then_inc(w_rest_in, 16)
            sp.dma_start(w2_sb[:, :, :], w2).then_inc(w_rest_in, 16)
            sp.dma_start(b2_sb[:, :], b2).then_inc(w_rest_in, 16)
            sp.dma_start(w3_sb[:, :], w3).then_inc(w_rest_in, 16)
            sp.wait_ge(y_copied, TILES)
            sp.dma_start(y, y_sb[:, :]).then_inc(y_out, 16)
            sp.wait_ge(y_out, 16)

        @block.gpsimd
        def _(pool):
            pool.wait_ge(ids_in, 16)
            for t in range(TILES):
                for g in range(GROUPS):
                    for slot in slots_of(g):
                        if slot == 0:
                            continue
                        at = t * TABLES + slot - 1
                        pool.indirect_dma_start(
                            out=rows[:, t, slot, :], out_offset=None, in_=tables[slot - 1],
                            in_offset=bass.IndirectOffsetOnAxis(ap=ids_sb[:, at:at + 1], axis=0),
                        ).then_inc(gathered[t][g], 16)

        def turned_to(t, g):
            own = slots_of(g)
            return features[:, t * P:(t + 1) * P, own.start:own.stop].rearrange("d s f -> d f s")

        def kept_run(t, run):
            start, stop, width = KEPT[run]
            out = kept[:, t % 2, KEPT_AT[run]:KEPT_AT[run + 1]].rearrange("s (m n) -> s m n", n=width)
            return out, products[:, start:stop, 0:width]

        def evacuated(count, parity):
            return (count + 1 - parity) // 2

        @block.tensor
        def _(pe):
            pe.wait_ge(eye_in, 16)
            pe.wait_ge(dense_in, 16)
            for t in range(TILES):
                for g in range(GROUPS):
                    i = t * GROUPS + g
                    gathers = sum(slot > 0 for slot in slots_of(g))
                    pe.wait_ge(gathered[t][g], 16 * gathers)
                    if i >= 2:
                        pe.wait_ge((features_act, features_dve)[i % 2], evacuated(i, i % 2))
                    for k, slot in enumerate(slots_of(g)):
                        last = nc.tensor.transpose(turned_ps[i % 2][:, k, :], rows[:, t, slot, :], eye[:, :])
                    last.then_inc(turned, 1)
                pe.wait_ge(features_act, evacuated((t + 1) * GROUPS, 0))
                pe.wait_ge(features_dve, evacuated((t + 1) * GROUPS, 1))
                if t == 0:
                    pe.wait_ge(gram_cleared, 1)
                else:
                    pe.wait_ge(products_done, t)
                for j in range(QUAD):
                    for q in range(P // QUAD):
                        sample = t * P + q * QUAD + j
                        last = nc.tensor.matmul(
                            gram_ps[q * QUAD:q * QUAD + SIDE, j, 0:SIDE],
                            features[:, sample, 0:SIDE], features[:, sample, 1:SLOTS],
                            start=True, stop=True)
                last.then_inc(gram_done, 1)
                pe.wait_ge(kept_dve, t + 1)
                pe.wait_ge(kept_act, t + 1)
                if t >= 1:
                    pe.wait_ge(pairs_copied, t)
                for k in range(PAIR_BLOCKS):
                    last = nc.tensor.transpose(pairs_ps[:, k, :], kept[:, t % 2, k * P:(k + 1) * P], eye[:, :])
                last.then_inc(pairs_turned, 1)
                if t == 0:
                    pe.wait_ge(w1_in, 32)
                    pe.wait_ge(w_dense_summed, 1)
                pe.wait_ge(pairs_copied, t + 1)
                for c in range(UNITS1):
                    units = slice(c * P, (c + 1) * P)
                    out = h1_ps[c // H1_HALF][:, c % H1_HALF, :]
                    nc.tensor.matmul(out, w_dense_sum[:, units],
                                     features[:, t * P:(t + 1) * P, 0], start=True, stop=False)
                    for k in range(PAIR_BLOCKS):
                        last = nc.tensor.matmul(out, w_pairs_sb[:, k, units], pairs[:, t % 2, k, :],
                                                start=False, stop=k == PAIR_BLOCKS - 1)
                    if c % H1_HALF == H1_HALF - 1:
                        last.then_inc(h1_done, 1)
                if t == 0:
                    pe.wait_ge(w_rest_in, 64)
                pe.wait_ge(h1_relu_act, t + 1)
                pe.wait_ge(h1_relu_dve, t + 1)
                if t >= 1:
                    pe.wait_ge(y_copied, t)
                for c in range(UNITS2):
                    for k in range(UNITS1):
                        last = nc.tensor.matmul(h2_ps[:, c, :], w2_sb[:, k, c * P:(c + 1) * P], h1[:, k, :],
                                                start=k == 0, stop=k == UNITS1 - 1)
                last.then_inc(h2_done, 1)
                pe.wait_ge(h2_relu, t + 1)
                for k in range(UNITS2):
                    last = nc.tensor.matmul(y_ps, w3_sb[:, k:k + 1], h2[:, k, :],
                                            start=k == 0, stop=k == UNITS2 - 1)
                last.then_inc(y_done, 1)

        @block.scalar
        def _(act):
            for t in range(TILES):
                for g in range(GROUPS):
                    i = t * GROUPS + g
                    if i % 2 == 0:
                        act.wait_ge(turned, i + 1)
                        nc.scalar.activation(turned_to(t, g), turned_ps[0][:, 0:len(slots_of(g)), :],
                                             ACT.Copy).then_inc(features_act, 1)
                act.wait_ge(products_done, t + 1)
                if t >= 2:
                    act.wait_ge(pairs_turned, t - 1)
                for run in range(KEPT_BY_VECTOR, len(KEPT)):
                    out, part = kept_run(t, run)
                    last = nc.scalar.activation(out, part, ACT.Copy)
                last.then_inc(kept_act, 1)
                act.wait_ge(pairs_turned, t + 1)
                if t >= 2:
                    act.wait_ge(h1_done, 2 * (t - 1))
                nc.scalar.activation(pairs[:, t % 2, :, :], pairs_ps[:, :, :], ACT.Copy).then_inc(pairs_copied, 1)
                if t == 0:
                    act.wait_ge(w_rest_in, 64)
                else:
                    act.wait_ge(h2_done, t)
                act.wait_ge(h1_done, 2 * t + 1)
                for c in range(H1_HALF):
                    last = nc.scalar.activation(h1[:, c, :], h1_ps[0][:, c, :], ACT.Relu, bias=b1_sb[:, c:c + 1])
                last.then_inc(h1_relu_act, 1)
                if t >= 1:
                    act.wait_ge(y_done, t)
                act.wait_ge(h2_done, t + 1)
                for c in range(UNITS2):
                    last = nc.scalar.activation(h2[:, c, :], h2_ps[:, c, :], ACT.Relu, bias=b2_sb[:, c:c + 1])
                last.then_inc(h2_relu, 1)
                act.wait_ge(y_done, t + 1)
                nc.scalar.activation(y_sb[0:1, t * P:(t + 1) * P], y_ps, ACT.Copy).then_inc(y_copied, 1)

        @block.vector
        def _(dve):
            nc.vector.memset(gram_ps[:, :, :], 0.0).then_inc(gram_cleared, 1)
            dve.wait_ge(w1_in, 32)
            nc.vector.tensor_tensor(w_dense_sum[:, :], w_dense_sb[:, 0, :], w_dense_sb[:, 1, :],
                                    ALU.add).then_inc(w_dense_summed, 1)
            for t in range(TILES):
                for g in range(GROUPS):
                    i = t * GROUPS + g
                    if i % 2 == 1:
                        dve.wait_ge(turned, i + 1)
                        nc.vector.tensor_copy(turned_to(t, g),
                                              turned_ps[1][:, 0:len(slots_of(g)), :]).then_inc(features_dve, 1)
                dve.wait_ge(gram_done, t + 1)
                if t >= 1:
                    dve.wait_ge(kept_act, t)
                nc.vector.transpose(products[:, :, :],
                                    gram_ps[:, :, 0:SIDE].rearrange("p s m -> p m s")).then_inc(products_done, 1)
                dve.wait_ge(products_done, t + 1)
                if t >= 2:
                    dve.wait_ge(pairs_turned, t - 1)
                for run in range(KEPT_BY_VECTOR):
                    out, part = kept_run(t, run)
                    last = nc.vector.tensor_copy(out, part)
                last.then_inc(kept_dve, 1)
                if t == 0:
                    dve.wait_ge(w_rest_in, 64)
                else:
                    dve.wait_ge(h2_done, t)
                dve.wait_ge(h1_done, 2 * t + 2)
                for c in range(H1_HALF, UNITS1):
                    last = nc.vector.tensor_scalar(h1[:, c, :], h1_ps[1][:, c - H1_HALF, :], b1_sb[:, c:c + 1],
                                                   0.0, ALU.add, ALU.max)
                last.then_inc(h1_relu_dve, 1)


def pairs_weights(w_top1, first_pair):
    out = np.zeros((PAIR_BLOCKS * P, w_top1.shape[1]), w_top1.dtype)
    at = 0
    for start, stop, width in KEPT:
        for m in range(start, stop):
            for n in range(width):
                if n <= m:
                    out[at] = w_top1[first_pair + n * SLOTS - n * (n + 1) // 2 + m - n]
                at += 1
    return out.reshape(PAIR_BLOCKS, P, -1).transpose(1, 0, 2)


def kernel(**inputs):
    import concourse.bacc as bacc
    from concourse.bass_utils import run_bass_kernel_spmd

    a = {name: np.asarray(value) for name, value in inputs.items()}
    batch, dim = a["r_dense_features"].shape
    w1 = a["W_top1"]
    hidden1, hidden2 = a["W_top2"].shape
    n_pairs = SLOTS * (SLOTS - 1) // 2

    def units_on_partitions(w):
        return w.reshape(w.shape[0] // P, P, -1).transpose(1, 0, 2)

    laid = {
        "dense": a["r_dense_features"],
        "ids": a["ids"].reshape(batch // P, P, TABLES).transpose(1, 0, 2).reshape(P, -1),
        **{f"table_{f}": a[f"tbl_{f}"] for f in range(TABLES)},
        "identity": np.eye(P, dtype=np.float32),
        "w_pairs": pairs_weights(w1, dim),
        "w_dense": np.stack([w1[:dim], w1[dim + n_pairs:]], axis=1),
        "b1": a["b_top1"].reshape(-1, P).T,
        "w2": units_on_partitions(a["W_top2"]),
        "b2": a["b_top2"].reshape(-1, P).T,
        "w3": units_on_partitions(a["W_top3"])[:, :, 0],
    }
    laid = {name: np.ascontiguousarray(value) for name, value in laid.items()}

    nc = bacc.Bacc("TRN2", target_bir_lowering=False, num_devices=1)
    d = {name: nc.dram_tensor(name, v.shape, mybir.dt.from_np(v.dtype), kind="ExternalInput").ap()
         for name, v in laid.items()}
    y = nc.dram_tensor("y", [1, batch], F32, kind="ExternalOutput").ap()
    dlrm_tower(nc, d["dense"], d["ids"], [d[f"table_{f}"] for f in range(TABLES)], d["identity"],
               d["w_pairs"], d["w_dense"], d["b1"], d["w2"], d["b2"], d["w3"], y)
    result = run_bass_kernel_spmd(nc, [laid], core_ids=[0])
    return result.results[0]["y"].reshape(batch, 1)
```

```python
from contextlib import ExitStack

import numpy as np

import concourse.bass as bass
from concourse import mybir

P = 128
TABLES = 26
SLOTS = TABLES + 1
SIDE = SLOTS - 1
QUAD = 32
PER_BANK = 4
PARTS = 3

ONE_HOT = [25, 23, 22, 21, 16]
LOOKUP_P = 125
LOOKUP_CHUNKS = 8
GROUPS = [(0, 4, 1), (4, 8, 1), (8, 12, 1), (12, 16, 1), (18, 22, 1), (16, 26, 9)]
GROUP_SLOTS = [list(range(*group)) for group in GROUPS]
ROW_SLOTS = sum(GROUP_SLOTS, [])
assert sorted(ROW_SLOTS + [f + 1 for f in ONE_HOT]) == list(range(SLOTS))

KEPT = [(0, 4, 4), (4, 8, 8), (8, 12, 12), (12, 16, 16), (16, 20, 20),
        (20, 22, 22), (22, 24, 24), (24, 25, 26), (25, 26, 26)]
KEPT_BY_VECTOR = 5
KEPT_AT = np.cumsum([0] + [(stop - start) * width for start, stop, width in KEPT]).tolist()
PAIR_BLOCKS = KEPT_AT[-1] // P
assert KEPT_AT[-1] == PAIR_BLOCKS * P

F32 = mybir.dt.float32
BF16 = mybir.dt.bfloat16
F16 = mybir.dt.float16
I32 = mybir.dt.int32
ALU = mybir.AluOpType
ACT = mybir.ActivationFunctionType


def order_of_steps(tiles):
    steps = [("one_hot", i, 0) for i in range(len(ONE_HOT))]
    ahead = {}
    for t in range(tiles):
        nxt = [("turn", t + 1, g) for g in range(len(GROUPS))] if t + 1 < tiles else []
        steps += [("turn", t, g) for g in range(ahead.get(t, 0), len(GROUPS))]
        take = FILL[t] if nxt else [0, 0, 0]
        steps += [("gram", t, 0)] + nxt[:take[0]]
        steps += [("pairs", t, 0)] + nxt[take[0]:take[1]]
        steps += [("layer1", t, 0)] + nxt[take[1]:take[2]]
        steps += [("layer2", t, 0), ("layer3", t, 0)]
        ahead[t + 1] = take[2]
    return steps


FILL = [(2, 3, 4), (2, 3, 4), (2, 3, 4)]


def dlrm_tower(nc, dense, ids, ids_by_table, row_numbers, tables, identity, w_pairs, w_dense,
               b1, w2, b2, w3, y):
    batch = dense.shape[0]
    hidden1, hidden2 = w_pairs.shape[2], w2.shape[2]
    TILES = batch // P
    UNITS1 = hidden1 // P
    UNITS2 = hidden2 // P
    H1_HALF = UNITS1 // 2
    STEPS = order_of_steps(TILES)
    TURN = {(t, g): i for i, (t, g) in enumerate((t, g) for what, t, g in STEPS if what == "turn")}
    assert all(tables[f].shape[0] == LOOKUP_P * LOOKUP_CHUNKS for f in ONE_HOT)

    with ExitStack() as ctx:
        def sb(name, shape, dt=F32):
            return ctx.enter_context(nc.sbuf_tensor(name, shape, dt))

        def psum(name, shape):
            return ctx.enter_context(nc.psum_tensor(name, shape, F32))

        def sem(name):
            return ctx.enter_context(nc.semaphore(name))

        ids_sb = sb("ids_sb", [P, TILES * TABLES], I32)
        rows = sb("rows", [P, TILES, len(ROW_SLOTS), P])
        eye = sb("eye", [P, P])
        features = sb("features", [P, batch, SLOTS])
        row_numbers_sb = sb("row_numbers_sb", [P, LOOKUP_CHUNKS])
        ids_spread = sb("ids_spread", [P, len(ONE_HOT), batch], I32)
        ids_half = sb("ids_half", [P, batch], F16)
        table_sb = sb("table_sb", [P, 2, LOOKUP_CHUNKS * P])
        table_parts = sb("table_parts", [P, 2, PARTS, LOOKUP_CHUNKS * P], BF16)
        table_rest = sb("table_rest", [P, LOOKUP_CHUNKS * P])
        chosen = sb("chosen", [P, 2, LOOKUP_CHUNKS, batch], BF16)
        products = sb("products", [P, SIDE, QUAD])
        kept = sb("kept", [P, 2, PAIR_BLOCKS * P])
        pairs = sb("pairs", [P, 2, PAIR_BLOCKS, P])
        w_pairs_sb = sb("w_pairs_sb", [P, PAIR_BLOCKS, hidden1])
        w_dense_sb = sb("w_dense_sb", [P, 2, hidden1])
        w_dense_sum = sb("w_dense_sum", [P, hidden1])
        b1_sb = sb("b1_sb", [P, UNITS1])
        w2_sb = sb("w2_sb", [P, UNITS1, hidden2])
        b2_sb = sb("b2_sb", [P, UNITS2])
        w3_sb = sb("w3_sb", [P, UNITS2])
        h1 = sb("h1", [P, UNITS1, P])
        h2 = sb("h2", [P, UNITS2, P])
        y_sb = sb("y_sb", [1, batch])

        turned_ps = [psum(f"turned_ps{i}", [P, PER_BANK, P]) for i in range(2)]
        gram_ps = psum("gram_ps", [P, 2, QUAD * QUAD // 2])
        gram = gram_ps[:, :, :].rearrange("p b (s m) -> p (b s) m", m=QUAD)
        lookup_ps = [gram_ps[:, i, :] for i in range(2)]
        pairs_ps = psum("pairs_ps", [P, PAIR_BLOCKS, P])
        h1_ps = [psum(f"h1_ps{i}", [P, UNITS1 // 2, P]) for i in range(2)]
        h2_y_ps = psum("h2_y_ps", [P, UNITS2 + 1, P])
        h2_ps = h2_y_ps[:, 0:UNITS2, :]
        y_ps = h2_y_ps[0:1, UNITS2, :]

        ids_in = sem("ids_in")
        eye_in = sem("eye_in")
        dense_in = sem("dense_in")
        w1_in = sem("w1_in")
        w_rest_in = sem("w_rest_in")
        row_numbers_in = sem("row_numbers_in")
        ids_spread_in = [sem(f"ids_spread_in{i}") for i in range(len(ONE_HOT))]
        table_in = [sem(f"table_in{i}") for i in range(2)]
        gathered = [[sem(f"gathered_{t}_{g}") for g in range(len(GROUPS))] for t in range(TILES)]
        ids_halved = sem("ids_halved")
        chosen_done = sem("chosen_done")
        hi_done = sem("hi_done")
        rest_done = sem("rest_done")
        mid_done = sem("mid_done")
        lo_done = sem("lo_done")
        looked_up = sem("looked_up")
        lookup_copied = sem("lookup_copied")
        w_dense_summed = sem("w_dense_summed")
        turned = sem("turned")
        features_act = sem("features_act")
        features_dve = sem("features_dve")
        gram_done = sem("gram_done")
        products_done = sem("products_done")
        kept_dve = sem("kept_dve")
        kept_act = sem("kept_act")
        pairs_turned = sem("pairs_turned")
        pairs_copied = sem("pairs_copied")
        h1_done = sem("h1_done")
        h1_relu_act = sem("h1_relu_act")
        h1_relu_dve = sem("h1_relu_dve")
        h2_done = sem("h2_done")
        h2_relu = sem("h2_relu")
        y_done = sem("y_done")
        y_copied = sem("y_copied")
        y_out = sem("y_out")

        def load_table(queue, i):
            by_partition = tables[ONE_HOT[i]].rearrange("(p c) d -> p (c d)", p=LOOKUP_P)
            for lo, hi in ((0, 112), (112, LOOKUP_P)):
                queue.dma_start(table_sb[lo:hi, i % 2, :], by_partition[lo:hi, :]).then_inc(table_in[i % 2], 16)

        def load_ids_spread(queue, i):
            queue.dma_start(ids_spread[:, i, :],
                            ids_by_table[i:i + 1, :].to_broadcast([P, batch])).then_inc(ids_spread_in[i], 16)

        def turned_to(t, g):
            first, stop, step = GROUPS[g]
            return features[:, t * P:(t + 1) * P, first:stop:step].rearrange("d s f -> d f s")

        def kept_run(t, run):
            start, stop, width = KEPT[run]
            out = kept[:, t % 2, KEPT_AT[run]:KEPT_AT[run + 1]].rearrange("s (m n) -> s m n", n=width)
            return out, products[:, start:stop, 0:width]

        def copies(count, parity):
            return (count + 1 - parity) // 2

        block = ctx.enter_context(nc.Block())

        @block.sync
        def _(sp):
            sp.dma_start(ids_sb[:, :], ids).then_inc(ids_in, 16)
            sp.dma_start(row_numbers_sb[:, :], row_numbers).then_inc(row_numbers_in, 16)
            load_ids_spread(sp, 1)
            load_table(sp, 1)
            sp.dma_start(eye[:, :], identity).then_inc(eye_in, 16)
            sp.dma_start(rows[:, :, 0, :], dense.rearrange("(t p) d -> p t d", p=P)).then_inc(dense_in, 16)
            for i in range(2, len(ONE_HOT)):
                load_ids_spread(sp, i)
                sp.wait_ge(rest_done, i - 1)
                load_table(sp, i)
            sp.dma_start(w_dense_sb[:, :, :], w_dense).then_inc(w1_in, 16)
            sp.dma_start(w_pairs_sb[:, :, :], w_pairs).then_inc(w1_in, 16)
            sp.dma_start(b1_sb[:, :], b1).then_inc(w_rest_in, 16)
            sp.dma_start(w2_sb[:, :, :], w2).then_inc(w_rest_in, 16)
            sp.dma_start(b2_sb[:, :], b2).then_inc(w_rest_in, 16)
            sp.dma_start(w3_sb[:, :], w3).then_inc(w_rest_in, 16)
            sp.wait_ge(y_copied, TILES)
            sp.dma_start(y, y_sb[:, :]).then_inc(y_out, 16)
            sp.wait_ge(y_out, 16)

        @block.gpsimd
        def _(pool):
            pool.wait_ge(ids_in, 16)
            for t in range(TILES):
                for g in range(len(GROUPS)):
                    for slot in GROUP_SLOTS[g]:
                        if slot == 0:
                            continue
                        at = t * TABLES + slot - 1
                        pool.indirect_dma_start(
                            out=rows[:, t, ROW_SLOTS.index(slot), :], out_offset=None, in_=tables[slot - 1],
                            in_offset=bass.IndirectOffsetOnAxis(ap=ids_sb[:, at:at + 1], axis=0),
                        ).then_inc(gathered[t][g], 16)

        @block.tensor
        def _(pe):
            def one_hot(i):
                b = i % 2
                if i >= 2:
                    pe.wait_ge(lookup_copied, i - 1)
                pe.wait_ge(chosen_done, i + 1)
                for part, ready in enumerate((hi_done, mid_done, lo_done)):
                    pe.wait_ge(ready, i + 1)
                    for c in range(LOOKUP_CHUNKS):
                        last = nc.tensor.matmul(
                            lookup_ps[b], table_parts[0:LOOKUP_P, b, part, c * P:(c + 1) * P],
                            chosen[0:LOOKUP_P, b, c, :],
                            start=part == 0 and c == 0, stop=part == PARTS - 1 and c == LOOKUP_CHUNKS - 1)
                last.then_inc(looked_up, 1)

            def turn(t, g):
                i = TURN[t, g]
                if i == 0:
                    pe.wait_ge(eye_in, 16)
                    pe.wait_ge(dense_in, 16)
                pe.wait_ge(gathered[t][g], 16 * sum(slot > 0 for slot in GROUP_SLOTS[g]))
                if i >= 2:
                    pe.wait_ge((features_act, features_dve)[i % 2], copies(i, i % 2))
                for k, slot in enumerate(GROUP_SLOTS[g]):
                    last = nc.tensor.transpose(turned_ps[i % 2][:, k, :], rows[:, t, ROW_SLOTS.index(slot), :],
                                               eye[:, :])
                last.then_inc(turned, 1)

            def gram_of(t):
                groups = 1 + max(TURN[t, g] for g in range(len(GROUPS)))
                pe.wait_ge(features_act, copies(groups, 0))
                pe.wait_ge(features_dve, copies(groups, 1))
                if t == 0:
                    pe.wait_ge(lookup_copied, len(ONE_HOT))
                else:
                    pe.wait_ge(products_done, t)
                for j in range(QUAD):
                    for q in range(P // QUAD):
                        sample = t * P + q * QUAD + j
                        last = nc.tensor.matmul(
                            gram[q * QUAD:q * QUAD + SIDE, j, 0:SIDE],
                            features[:, sample, 0:SIDE], features[:, sample, 1:SLOTS],
                            start=True, stop=True)
                last.then_inc(gram_done, 1)

            def turn_pairs(t):
                pe.wait_ge(kept_dve, t + 1)
                pe.wait_ge(kept_act, t + 1)
                if t >= 1:
                    pe.wait_ge(pairs_copied, t)
                for k in range(PAIR_BLOCKS):
                    last = nc.tensor.transpose(pairs_ps[:, k, :], kept[:, t % 2, k * P:(k + 1) * P], eye[:, :])
                last.then_inc(pairs_turned, 1)

            def layer1(t):
                if t == 0:
                    pe.wait_ge(w1_in, 32)
                    pe.wait_ge(w_dense_summed, 1)
                else:
                    pe.wait_ge(h1_relu_act, t)
                    pe.wait_ge(h1_relu_dve, t)
                pe.wait_ge(pairs_copied, t + 1)
                for c in range(UNITS1):
                    units = slice(c * P, (c + 1) * P)
                    out = h1_ps[c // H1_HALF][:, c % H1_HALF, :]
                    nc.tensor.matmul(out, w_dense_sum[:, units],
                                     features[:, t * P:(t + 1) * P, 0], start=True, stop=False)
                    for k in range(PAIR_BLOCKS):
                        last = nc.tensor.matmul(out, w_pairs_sb[:, k, units], pairs[:, t % 2, k, :],
                                                start=False, stop=k == PAIR_BLOCKS - 1)
                    if c % H1_HALF == H1_HALF - 1:
                        last.then_inc(h1_done, 1)

            def layer2(t):
                if t == 0:
                    pe.wait_ge(w_rest_in, 64)
                else:
                    pe.wait_ge(y_copied, t)
                pe.wait_ge(h1_relu_act, t + 1)
                pe.wait_ge(h1_relu_dve, t + 1)
                for c in range(UNITS2):
                    for k in range(UNITS1):
                        last = nc.tensor.matmul(h2_ps[:, c, :], w2_sb[:, k, c * P:(c + 1) * P], h1[:, k, :],
                                                start=k == 0, stop=k == UNITS1 - 1)
                last.then_inc(h2_done, 1)

            def layer3(t):
                pe.wait_ge(h2_relu, t + 1)
                for k in range(UNITS2):
                    last = nc.tensor.matmul(y_ps, w3_sb[:, k:k + 1], h2[:, k, :],
                                            start=k == 0, stop=k == UNITS2 - 1)
                last.then_inc(y_done, 1)

            for what, t, g in STEPS:
                if what == "one_hot":
                    one_hot(t)
                elif what == "turn":
                    turn(t, g)
                elif what == "gram":
                    gram_of(t)
                elif what == "pairs":
                    turn_pairs(t)
                elif what == "layer1":
                    layer1(t)
                elif what == "layer2":
                    layer2(t)
                else:
                    layer3(t)

        @block.scalar
        def _(act):
            load_ids_spread(act, 0)
            load_table(act, 0)

            def split_table(i):
                b = i % 2
                act.wait_ge(table_in[b], 32 * (i // 2 + 1))
                if i >= 2:
                    act.wait_ge(looked_up, i - 1)
                nc.scalar.activation(table_parts[0:LOOKUP_P, b, 0, :], table_sb[0:LOOKUP_P, b, :],
                                     ACT.Copy).then_inc(hi_done, 1)
                act.wait_ge(rest_done, i + 1)
                nc.scalar.activation(table_parts[0:LOOKUP_P, b, 1, :], table_rest[0:LOOKUP_P, :],
                                     ACT.Copy).then_inc(mid_done, 1)

            split_table(0)
            for what, t, g in STEPS:
                if what == "one_hot":
                    if t + 1 < len(ONE_HOT):
                        split_table(t + 1)
                    act.wait_ge(looked_up, t + 1)
                    nc.scalar.activation(features[:, :, ONE_HOT[t] + 1], lookup_ps[t % 2],
                                         ACT.Copy).then_inc(lookup_copied, 1)
                elif what == "turn" and TURN[t, g] % 2 == 0:
                    act.wait_ge(turned, TURN[t, g] + 1)
                    nc.scalar.activation(turned_to(t, g), turned_ps[0][:, 0:len(GROUP_SLOTS[g]), :],
                                         ACT.Copy).then_inc(features_act, 1)
                elif what == "gram":
                    act.wait_ge(products_done, t + 1)
                    if t >= 2:
                        act.wait_ge(pairs_turned, t - 1)
                    for run in range(KEPT_BY_VECTOR, len(KEPT)):
                        out, part = kept_run(t, run)
                        last = nc.scalar.activation(out, part, ACT.Copy)
                    last.then_inc(kept_act, 1)
                elif what == "pairs":
                    act.wait_ge(pairs_turned, t + 1)
                    if t >= 2:
                        act.wait_ge(h1_done, 2 * (t - 1))
                    nc.scalar.activation(pairs[:, t % 2, :, :], pairs_ps[:, :, :], ACT.Copy).then_inc(pairs_copied, 1)
                elif what == "layer1":
                    if t == 0:
                        act.wait_ge(w_rest_in, 64)
                    else:
                        act.wait_ge(h2_done, t)
                    act.wait_ge(h1_done, 2 * t + 1)
                    for c in range(H1_HALF):
                        last = nc.scalar.activation(h1[:, c, :], h1_ps[0][:, c, :], ACT.Relu, bias=b1_sb[:, c:c + 1])
                    last.then_inc(h1_relu_act, 1)
                elif what == "layer2":
                    if t >= 1:
                        act.wait_ge(y_done, t)
                    act.wait_ge(h2_done, t + 1)
                    for c in range(UNITS2):
                        last = nc.scalar.activation(h2[:, c, :], h2_ps[:, c, :], ACT.Relu, bias=b2_sb[:, c:c + 1])
                    last.then_inc(h2_relu, 1)
                elif what == "layer3":
                    act.wait_ge(y_done, t + 1)
                    nc.scalar.activation(y_sb[0:1, t * P:(t + 1) * P], y_ps, ACT.Copy).then_inc(y_copied, 1)

        @block.vector
        def _(dve):
            def choose_and_split(i):
                b = i % 2
                dve.wait_ge(ids_spread_in[i], 16)
                if i >= 1:
                    dve.wait_ge(chosen_done, i)
                nc.vector.tensor_copy(ids_half[0:LOOKUP_P, :], ids_spread[0:LOOKUP_P, i, :]).then_inc(ids_halved, 1)
                dve.wait_ge(ids_halved, i + 1)
                if i == 0:
                    dve.wait_ge(row_numbers_in, 16)
                if i >= 2:
                    dve.wait_ge(looked_up, i - 1)
                for c in range(LOOKUP_CHUNKS):
                    last = nc.vector.tensor_scalar(chosen[0:LOOKUP_P, b, c, :], ids_half[0:LOOKUP_P, :],
                                                   row_numbers_sb[0:LOOKUP_P, c:c + 1], None, ALU.is_equal)
                last.then_inc(chosen_done, 1)
                dve.wait_ge(hi_done, i + 1)
                if i >= 1:
                    dve.wait_ge(lo_done, i)
                nc.vector.tensor_tensor(table_rest[0:LOOKUP_P, :], table_sb[0:LOOKUP_P, b, :],
                                        table_parts[0:LOOKUP_P, b, 0, :], ALU.subtract).then_inc(rest_done, 1)
                dve.wait_ge(mid_done, i + 1)
                nc.vector.tensor_tensor(table_parts[0:LOOKUP_P, b, 2, :], table_rest[0:LOOKUP_P, :],
                                        table_parts[0:LOOKUP_P, b, 1, :], ALU.subtract).then_inc(lo_done, 1)

            choose_and_split(0)
            for what, t, g in STEPS:
                if what == "one_hot":
                    if t + 1 < len(ONE_HOT):
                        choose_and_split(t + 1)
                    else:
                        dve.wait_ge(w1_in, 32)
                        nc.vector.tensor_tensor(w_dense_sum[:, :], w_dense_sb[:, 0, :], w_dense_sb[:, 1, :],
                                                ALU.add).then_inc(w_dense_summed, 1)
                elif what == "turn" and TURN[t, g] % 2 == 1:
                    dve.wait_ge(turned, TURN[t, g] + 1)
                    nc.vector.tensor_copy(turned_to(t, g),
                                          turned_ps[1][:, 0:len(GROUP_SLOTS[g]), :]).then_inc(features_dve, 1)
                elif what == "gram":
                    dve.wait_ge(gram_done, t + 1)
                    if t >= 1:
                        dve.wait_ge(kept_act, t)
                        dve.wait_ge(kept_dve, t)
                    nc.vector.transpose(products[:, :, :],
                                        gram[:, :, 0:SIDE].rearrange("p s m -> p m s")).then_inc(products_done, 1)
                    dve.wait_ge(products_done, t + 1)
                    if t >= 2:
                        dve.wait_ge(pairs_turned, t - 1)
                    for run in range(KEPT_BY_VECTOR):
                        out, part = kept_run(t, run)
                        last = nc.vector.tensor_copy(out, part)
                    last.then_inc(kept_dve, 1)
                elif what == "layer1":
                    if t == 0:
                        dve.wait_ge(w_rest_in, 64)
                    else:
                        dve.wait_ge(h2_done, t)
                    dve.wait_ge(h1_done, 2 * t + 2)
                    for c in range(H1_HALF, UNITS1):
                        last = nc.vector.tensor_scalar(h1[:, c, :], h1_ps[1][:, c - H1_HALF, :], b1_sb[:, c:c + 1],
                                                       0.0, ALU.add, ALU.max)
                    last.then_inc(h1_relu_dve, 1)


def pairs_weights(w_top1, first_pair):
    out = np.zeros((PAIR_BLOCKS * P, w_top1.shape[1]), w_top1.dtype)
    at = 0
    for start, stop, width in KEPT:
        for m in range(start, stop):
            for n in range(width):
                if n <= m:
                    out[at] = w_top1[first_pair + n * SLOTS - n * (n + 1) // 2 + m - n]
                at += 1
    return out.reshape(PAIR_BLOCKS, P, -1).transpose(1, 0, 2)


def kernel(**inputs):
    import concourse.bacc as bacc
    from concourse.bass_utils import run_bass_kernel_spmd

    a = {name: np.asarray(value) for name, value in inputs.items()}
    batch, dim = a["r_dense_features"].shape
    w1 = a["W_top1"]
    n_pairs = SLOTS * (SLOTS - 1) // 2

    def units_on_partitions(w):
        return w.reshape(w.shape[0] // P, P, -1).transpose(1, 0, 2)

    laid = {
        "dense": a["r_dense_features"],
        "ids": a["ids"].reshape(batch // P, P, TABLES).transpose(1, 0, 2).reshape(P, -1),
        "ids_by_table": a["ids"][:, ONE_HOT].T,
        "row_numbers": np.arange(P * LOOKUP_CHUNKS, dtype=np.float32).reshape(P, LOOKUP_CHUNKS),
        **{f"table_{f}": a[f"tbl_{f}"] for f in range(TABLES)},
        "identity": np.eye(P, dtype=np.float32),
        "w_pairs": pairs_weights(w1, dim),
        "w_dense": np.stack([w1[:dim], w1[dim + n_pairs:]], axis=1),
        "b1": a["b_top1"].reshape(-1, P).T,
        "w2": units_on_partitions(a["W_top2"]),
        "b2": a["b_top2"].reshape(-1, P).T,
        "w3": units_on_partitions(a["W_top3"])[:, :, 0],
    }
    laid = {name: np.ascontiguousarray(value) for name, value in laid.items()}

    nc = bacc.Bacc("TRN2", target_bir_lowering=False, num_devices=1)
    d = {name: nc.dram_tensor(name, v.shape, mybir.dt.from_np(v.dtype), kind="ExternalInput").ap()
         for name, v in laid.items()}
    y = nc.dram_tensor("y", [1, batch], F32, kind="ExternalOutput").ap()
    dlrm_tower(nc, d["dense"], d["ids"], d["ids_by_table"], d["row_numbers"],
               [d[f"table_{f}"] for f in range(TABLES)], d["identity"],
               d["w_pairs"], d["w_dense"], d["b1"], d["w2"], d["b2"], d["w3"], y)
    result = run_bass_kernel_spmd(nc, [laid], core_ids=[0])
    return result.results[0]["y"].reshape(batch, 1)
```

```python
from contextlib import ExitStack

import numpy as np

import concourse.bass as bass
from concourse import mybir

P = 128
TABLES = 26
SLOTS = TABLES + 1
SIDE = SLOTS - 1
QUAD = 32
PER_BANK = 4
PARTS = 3

ONE_HOT = [23, 22, 21, 16, 15, 14, 25]
WHOLE_LOOKUPS = 4
EARLY_LOOKUPS = 6
LOOKUP_P = 125
LOOKUP_CHUNKS = 8
BUFFERS = 3
TILE_GROUPS = [(0, 4), (4, 8), (8, 12), (12, 15), (18, 22)]
LAST_TILE_GROUPS = [(0, 1), (25, 26)]
HALF_GROUPS = [(1, 9), (9, 15), (18, 20), (20, 22)]

KEPT = [(0, 4, 4), (4, 8, 8), (8, 12, 12), (12, 16, 16), (16, 20, 20),
        (20, 22, 22), (22, 24, 24), (24, 25, 26), (25, 26, 26)]
KEPT_BY_VECTOR = 3
PIECES = [(slice(20, SIDE), range(5, 9)), (slice(12, 20), range(3, 5)), (slice(0, 12), range(0))]
KEPT_AT = np.cumsum([0] + [(stop - start) * width for start, stop, width in KEPT]).tolist()
PAIR_BLOCKS = KEPT_AT[-1] // P
assert [run for _, runs in PIECES[::-1] for run in runs] == list(range(KEPT_BY_VECTOR, len(KEPT)))
assert KEPT_AT[-1] == PAIR_BLOCKS * P

F32 = mybir.dt.float32
BF16 = mybir.dt.bfloat16
F16 = mybir.dt.float16
I32 = mybir.dt.int32
ALU = mybir.AluOpType
ACT = mybir.ActivationFunctionType


class Span:

    def __init__(self, tile, late, half=None):
        self.tile, self.half = tile, half
        self.partitions = slice(0, P) if half is None else slice(half * P // 2, (half + 1) * P // 2)
        self.samples = slice(tile * P + self.partitions.start, tile * P + self.partitions.stop)
        self.quads = range(self.partitions.start // QUAD, self.partitions.stop // QUAD)
        self.groups = []
        if half is None:
            last = (25, 26) if late else (25, 27)
            self.groups += [(*slots, self.samples, 1) for slots in TILE_GROUPS + [last]]
        if half == 0:
            self.groups += [(*slots, slice(tile * P, (tile + 1) * P), 1) for slots in LAST_TILE_GROUPS]
        if half is not None:
            self.groups += [(*slots, self.samples, 2) for slots in HALF_GROUPS]


def spans_of(batch):
    tiles = batch // P
    return [Span(t, t >= tiles // 2) for t in range(tiles - 1)] + [Span(tiles - 1, True, half) for half in (0, 1)]


ORDER = """
    busy 50, lookup 0, lookup 1, lookup 2, lookup 3, lookup 4, lookup 5,
    turn 0.0, turn 0.1, late 4.0, turn 0.2, turn 0.3, late 4.1, turn 0.4, turn 0.5, late 4.2,
    hi 6, gram 0, turn 1.0, turn 1.1, late 5.0, dense 0, pairs 0, turn 1.2, layer1 0, layer2 0,
    turn 1.3, turn 1.4, late 5.1, layer3 0, turn 1.5, late 5.2,
    mid 6, lo 6, gram 1, turn 2.0, turn 2.1, late 6.0, dense 1, pairs 1, turn 2.2, layer1 1,
    turn 2.3, layer2 1, turn 2.4, late 6.1, late 6.2, turn 2.5, layer3 1, busy 8,
    gram 2, dense 2, turn 3.2, busy 10, pairs 2, turn 3.0, turn 3.1, busy 7, layer1 2,
    turn 3.3, layer2 2, turn 3.4, turn 3.5, busy 12,
    gram 3, layer3 2, turn 4.0, turn 4.1, busy 12, pairs 3, turn 4.2, busy 3, turn 4.3, busy 7,
    gram 4, dense 3, busy 14, pairs 4, busy 6, layer1 3, layer2 3, busy 12, layer3 3
"""


def steps_in(order):
    for step in order.split(","):
        what, which = step.split()
        first, _, second = which.partition(".")
        yield what, int(first), int(second or 0)


def gathers_of(spans):
    for u, span in enumerate(spans):
        for g, (first, stop, samples, at_once) in enumerate(span.groups):
            for slot in range(max(first, 1), stop, at_once):
                yield u, g, samples, range(slot, slot + at_once)


def dlrm_tower(nc, dense, ids_and_bases, ids_by_table, constants, tables, lookup_bases, w_pairs, w_dense,
               b1, w2, b2, w3, y):
    batch = dense.shape[0]
    hidden1, hidden2 = w_pairs.shape[2], w2.shape[2]
    TILES = batch // P
    UNITS1 = hidden1 // P
    UNITS2 = hidden2 // P
    H1_HALF = UNITS1 // 2
    assert UNITS2 == 2
    SPANS = spans_of(batch)
    STEPS = list(steps_in(ORDER))
    GATHERS = list(gathers_of(SPANS))
    LATE_SAMPLES = slice(batch // 2, batch)
    EARLY_SAMPLES = [slice(0, batch if i < WHOLE_LOOKUPS else LATE_SAMPLES.start) for i in range(EARLY_LOOKUPS)]
    SPANS_TO = [sum(span.tile <= t for span in SPANS) for t in range(TILES)]
    TURN = {(u, g): i for i, (u, g) in enumerate((u, g) for what, u, g in STEPS if what == "turn")}

    with ExitStack() as ctx:
        def sb(name, shape, dt=F32):
            return ctx.enter_context(nc.sbuf_tensor(name, shape, dt))

        def psum(name, shape):
            return ctx.enter_context(nc.psum_tensor(name, shape, F32))

        def sem(name):
            return ctx.enter_context(nc.semaphore(name))

        ids_sb = sb("ids_sb", [P, 2, len(GATHERS)], I32)
        row_at = sb("row_at", [P, len(GATHERS)], I32)
        dense_sb = sb("dense_sb", [P, TILES, P])
        rows = sb("rows", [P, len(GATHERS), P])
        constants_sb = sb("constants_sb", [P, P + LOOKUP_CHUNKS])
        eye = constants_sb[:, 0:P]
        row_numbers = constants_sb[:, P:P + LOOKUP_CHUNKS]
        features = sb("features", [P, batch, SLOTS])
        ids_spread = sb("ids_spread", [P, len(ONE_HOT), batch], I32)
        ids_half = sb("ids_half", [P, 2, batch], F16)
        table_sb = sb("table_sb", [P, 2, LOOKUP_CHUNKS * P])
        table_parts = sb("table_parts", [P, BUFFERS, PARTS, LOOKUP_CHUNKS * P], BF16)
        table_rest = sb("table_rest", [P, LOOKUP_CHUNKS * P])
        chosen = sb("chosen", [P, BUFFERS, LOOKUP_CHUNKS, batch], BF16)
        zeros = sb("zeros", [P, P], BF16)
        products = sb("products", [P, SIDE, QUAD])
        kept = sb("kept", [P, 2, PAIR_BLOCKS * P])
        pairs = sb("pairs", [P, 2, PAIR_BLOCKS, P])
        w_pairs_sb = sb("w_pairs_sb", [P, PAIR_BLOCKS, hidden1])
        w_dense_sb = sb("w_dense_sb", [P, 2, hidden1])
        w_dense_sum = sb("w_dense_sum", [P, hidden1])
        b1_sb = sb("b1_sb", [P, UNITS1])
        w2_sb = sb("w2_sb", [P, UNITS1, hidden2])
        b2_sb = sb("b2_sb", [P, UNITS2])
        w3_sb = sb("w3_sb", [P, UNITS2])
        h1 = sb("h1", [P, UNITS1, P])
        h2 = sb("h2", [P, UNITS2, P])
        y_sb = sb("y_sb", [P, TILES])

        turned_ps = [psum(f"turned_ps{i}", [P, PER_BANK * P]) for i in range(2)]
        gram_ps = psum("gram_ps", [P, 2, QUAD * QUAD // 2])
        gram = gram_ps[:, :, :].rearrange("p b (s m) -> p (b s) m", m=QUAD)
        lookup_ps = [gram_ps[:, i, :] for i in range(2)]
        pairs_bank = psum("pairs_bank", [P, PER_BANK, P])
        pairs_ps = pairs_bank[:, 0:PAIR_BLOCKS, :]
        h1_ps = [psum(f"h1_ps{i}", [P, UNITS1 // 2, P]) for i in range(2)]
        h2_ps = [h1_ps[0][:, 0, :], pairs_bank[:, PAIR_BLOCKS, :]]
        y_ps = h1_ps[1][:, 0, 0:1]
        late_bank = psum("late_bank", [P, PER_BANK * P])
        late_ps = late_bank[:, 0:batch - LATE_SAMPLES.start]
        idle_ps = late_bank[:, PER_BANK * P - P:PER_BANK * P]

        ids_in = sem("ids_in")
        constants_in = sem("constants_in")
        dense_in = sem("dense_in")
        w1_in = sem("w1_in")
        w_rest_in = sem("w_rest_in")
        ids_spread_in = [sem(f"ids_spread_in{i}") for i in range(len(ONE_HOT))]
        table_in = [sem(f"table_in{i}") for i in range(2)]
        gathered = [[sem(f"gathered_{u}_{g}") for g in range(len(span.groups))] for u, span in enumerate(SPANS)]
        row_at_done = sem("row_at_done")
        zeros_set = sem("zeros_set")
        ids_halved = sem("ids_halved")
        chosen_done = sem("chosen_done")
        hi_done = sem("hi_done")
        rest_done = sem("rest_done")
        mid_done = sem("mid_done")
        lo_done = sem("lo_done")
        looked_up = sem("looked_up")
        lookup_copied = sem("lookup_copied")
        looked_up_late = sem("looked_up_late")
        late_copied = sem("late_copied")
        w_dense_summed = sem("w_dense_summed")
        turned = sem("turned")
        features_act = sem("features_act")
        features_dve = sem("features_dve")
        gram_done = sem("gram_done")
        products_done = sem("products_done")
        kept_dve = sem("kept_dve")
        kept_act = sem("kept_act")
        pairs_turned = sem("pairs_turned")
        pairs_copied = sem("pairs_copied")
        h1_done = sem("h1_done")
        h1_relu_act = sem("h1_relu_act")
        h1_relu_dve = sem("h1_relu_dve")
        h2_done = sem("h2_done")
        h2_relu_act = sem("h2_relu_act")
        h2_relu_dve = sem("h2_relu_dve")
        y_done = sem("y_done")
        y_copied = sem("y_copied")
        y_out = sem("y_out")

        def load_table(queue, i):
            first = lookup_bases[i]
            table = tables[first:first + LOOKUP_P * LOOKUP_CHUNKS, :]
            by_partition = table.rearrange("(p c) d -> p (c d)", p=LOOKUP_P)
            for lo, hi in ((0, 112), (112, LOOKUP_P)):
                queue.dma_start(table_sb[lo:hi, i % 2, :], by_partition[lo:hi, :]).then_inc(table_in[i % 2], 16)

        def load_ids_spread(queue, i):
            queue.dma_start(ids_spread[:, i, :],
                            ids_by_table[i:i + 1, :].to_broadcast([P, batch])).then_inc(ids_spread_in[i], 16)

        def blocks(u, g):
            dense_block = [dense_sb[:, SPANS[u].tile, :]] if SPANS[u].groups[g][0] == 0 else []
            return dense_block + [rows[:, i, :] for i, (v, h, _, _) in enumerate(GATHERS) if (v, h) == (u, g)]

        def copy_of_turned(u, g):
            first, stop, samples, _ = SPANS[u].groups[g]
            size = samples.stop - samples.start
            here = turned_ps[TURN[u, g] % 2][:, 0:(stop - first) * size]
            return (features[:, samples, first:stop].rearrange("d s f -> d f s"),
                    here.rearrange("d (f s) -> d f s", s=size))

        def kept_run(u, run):
            start, stop, width = KEPT[run]
            out = kept[SPANS[u].partitions, u % 2, KEPT_AT[run]:KEPT_AT[run + 1]]
            return out.rearrange("s (m n) -> s m n", n=width), products[SPANS[u].partitions, start:stop, 0:width]

        def copies(count, parity):
            return (count + 1 - parity) // 2

        block = ctx.enter_context(nc.Block())

        @block.sync
        def _(sp):
            sp.dma_start(ids_sb[:, :, :], ids_and_bases).then_inc(ids_in, 16)
            load_ids_spread(sp, 0)
            sp.dma_start(constants_sb[:, :], constants).then_inc(constants_in, 16)
            load_table(sp, 0)
            load_table(sp, 1)
            load_ids_spread(sp, 1)
            sp.dma_start(dense_sb[:, :, :], dense.rearrange("(t p) d -> p t d", p=P)).then_inc(dense_in, 16)
            for i in range(2, len(ONE_HOT)):
                load_ids_spread(sp, i)
                sp.wait_ge(rest_done, i - 1)
                load_table(sp, i)
            sp.dma_start(w_dense_sb[:, :, :], w_dense).then_inc(w1_in, 16)
            sp.dma_start(w_pairs_sb[:, :, :], w_pairs).then_inc(w1_in, 16)
            sp.dma_start(b1_sb[:, :], b1).then_inc(w_rest_in, 16)
            sp.dma_start(w2_sb[:, :, :], w2).then_inc(w_rest_in, 16)
            sp.dma_start(b2_sb[:, :], b2).then_inc(w_rest_in, 16)
            sp.dma_start(w3_sb[:, :], w3).then_inc(w_rest_in, 16)
            sp.wait_ge(y_copied, TILES)
            sp.dma_start(y, y_sb[:, :]).then_inc(y_out, 16)
            sp.wait_ge(y_out, 16)

        @block.gpsimd
        def _(pool):
            assert GATHERS[0][3][0] == 1
            pool.wait_ge(ids_in, 16)
            for i, (u, g, _, _) in enumerate(GATHERS):
                if i == 1:
                    pool.wait_ge(row_at_done, 1)
                row_ids = ids_sb[:, 0, 0:1] if i == 0 else row_at[:, i:i + 1]
                pool.indirect_dma_start(
                    out=rows[:, i, :], out_offset=None, in_=tables,
                    in_offset=bass.IndirectOffsetOnAxis(ap=row_ids, axis=0),
                ).then_inc(gathered[u][g], 16)

        @block.tensor
        def _(pe):
            def lookup_part(out, i, part, samples, as_chosen=False):
                for c in range(LOOKUP_CHUNKS):
                    if as_chosen:
                        pe.wait_ge(chosen_done, i * LOOKUP_CHUNKS + c + 1)
                    last = nc.tensor.matmul(
                        out, table_parts[0:LOOKUP_P, i % BUFFERS, part, c * P:(c + 1) * P],
                        chosen[0:LOOKUP_P, i % BUFFERS, c, samples],
                        start=part == 0 and c == 0, stop=part == PARTS - 1 and c == LOOKUP_CHUNKS - 1)
                return last

            def lookup(i):
                if i >= 2:
                    pe.wait_ge(lookup_copied, i - 1)
                samples = EARLY_SAMPLES[i]
                for part, ready in enumerate((hi_done, mid_done, lo_done)):
                    pe.wait_ge(ready, i + 1)
                    last = lookup_part(lookup_ps[i % 2][:, samples], i, part, samples, as_chosen=part == 0)
                last.then_inc(looked_up, 1)

            def late_lookup(i, part):
                if i > WHOLE_LOOKUPS and part == 0:
                    pe.wait_ge(late_copied, i - WHOLE_LOOKUPS)
                if i >= EARLY_LOOKUPS:
                    pe.wait_ge((hi_done, mid_done, lo_done)[part], i + 1)
                last = lookup_part(late_ps, i, part, LATE_SAMPLES, as_chosen=i >= EARLY_LOOKUPS and part == 0)
                if part == PARTS - 1:
                    last.then_inc(looked_up_late, 1)

            def turn(u, g):
                i = TURN[u, g]
                if i == 0:
                    pe.wait_ge(constants_in, 16)
                    pe.wait_ge(dense_in, 16)
                gathers = sum((v, h) == (u, g) for v, h, _, _ in GATHERS)
                if gathers:
                    pe.wait_ge(gathered[u][g], 16 * gathers)
                if i >= 2:
                    pe.wait_ge((features_act, features_dve)[i % 2], copies(i, i % 2))
                for k, block_in in enumerate(blocks(u, g)):
                    last = nc.tensor.transpose(turned_ps[i % 2][:, k * P:(k + 1) * P], block_in, eye)
                last.then_inc(turned, 1)

            def gram_of(u):
                span = SPANS[u]
                groups = 1 + max(TURN[u, g] for g in range(len(span.groups)))
                pe.wait_ge(features_act, copies(groups, 0))
                pe.wait_ge(features_dve, copies(groups, 1))
                if u == 0:
                    pe.wait_ge(lookup_copied, EARLY_LOOKUPS)
                if LATE_SAMPLES.start == span.samples.start:
                    pe.wait_ge(late_copied, len(ONE_HOT) - WHOLE_LOOKUPS)
                if u >= 1:
                    pe.wait_ge(products_done, len(PIECES) * (u - (span.half == 1)))
                for j in range(QUAD):
                    for q in span.quads:
                        sample = span.tile * P + q * QUAD + j
                        last = nc.tensor.matmul(
                            gram[q * QUAD:q * QUAD + SIDE, j, 0:SIDE],
                            features[:, sample, 0:SIDE], features[:, sample, 1:SLOTS],
                            start=True, stop=True)
                last.then_inc(gram_done, 1)

            def turn_pairs(u):
                own = SPANS[u].partitions
                if u >= 1:
                    pe.wait_ge(pairs_copied, PAIR_BLOCKS * u)
                if SPANS[u].tile >= 1:
                    pe.wait_ge(h2_relu_dve, SPANS[u].tile)
                pe.wait_ge(kept_act, u + 1)
                pe.wait_ge(kept_dve, u + 1)
                for k in range(PAIR_BLOCKS):
                    last = nc.tensor.transpose(pairs_ps[:, k, own], kept[own, u % 2, k * P:(k + 1) * P],
                                               eye[own, own])
                last.then_inc(pairs_turned, 1)

            def layer1_dense(t):
                if t == 0:
                    pe.wait_ge(w1_in, 32)
                    pe.wait_ge(w_dense_summed, 1)
                else:
                    pe.wait_ge(h2_relu_act, t)
                    pe.wait_ge(y_copied, t)
                for c in range(UNITS1):
                    nc.tensor.matmul(h1_ps[c // H1_HALF][:, c % H1_HALF, :], w_dense_sum[:, c * P:(c + 1) * P],
                                     features[:, t * P:(t + 1) * P, 0], start=c % H1_HALF == 0, stop=False,
                                     skip_group_check=True)

            def layer1(t):
                for half in range(2):
                    for k in range(PAIR_BLOCKS):
                        if half == 0:
                            pe.wait_ge(pairs_copied, PAIR_BLOCKS * (SPANS_TO[t] - 1) + k + 1)
                        for c in range(half * H1_HALF, (half + 1) * H1_HALF):
                            last = nc.tensor.matmul(h1_ps[half][:, c % H1_HALF, :],
                                                    w_pairs_sb[:, k, c * P:(c + 1) * P], pairs[:, t % 2, k, :],
                                                    start=False, stop=k == PAIR_BLOCKS - 1, skip_group_check=True)
                    last.then_inc(h1_done, 1)

            def layer2(t):
                if t == 0:
                    pe.wait_ge(w_rest_in, 64)
                for half, ready in enumerate((h1_relu_act, h1_relu_dve)):
                    for c in range(UNITS2):
                        for k in range(half * H1_HALF, (half + 1) * H1_HALF):
                            if c == 0:
                                blocks_ready = H1_HALF if half == 0 else k % H1_HALF + 1
                                pe.wait_ge(ready, t * H1_HALF + blocks_ready)
                            last = nc.tensor.matmul(h2_ps[c], w2_sb[:, k, c * P:(c + 1) * P],
                                                    h1[:, k, :], start=k == 0, stop=k == UNITS1 - 1)
                last.then_inc(h2_done, 1)

            def layer3(t):
                for k, ready in enumerate((h2_relu_act, h2_relu_dve)):
                    pe.wait_ge(ready, t + 1)
                    last = nc.tensor.matmul(y_ps, h2[:, k, :], w3_sb[:, k:k + 1],
                                            start=k == 0, stop=k == UNITS2 - 1)
                last.then_inc(y_done, 1)

            def stay_busy(products, late_lookups):
                pe.wait_ge(zeros_set, 1)
                if late_lookups:
                    pe.wait_ge(late_copied, late_lookups)
                for _ in range(products):
                    nc.tensor.matmul(idle_ps, zeros[:, :], zeros[:, :], start=True, stop=True)

            for step, (what, t, g) in enumerate(STEPS):
                if what == "lookup":
                    lookup(t)
                elif what == "late":
                    late_lookup(t, g)
                elif what == "dense":
                    layer1_dense(t)
                elif what in ("hi", "mid", "lo"):
                    pass
                elif what == "busy":
                    stay_busy(t, sum(before == "late" and part == PARTS - 1 for before, _, part in STEPS[:step]))
                elif what == "turn":
                    turn(t, g)
                elif what == "gram":
                    gram_of(t)
                elif what == "pairs":
                    turn_pairs(t)
                elif what == "layer1":
                    layer1(t)
                elif what == "layer2":
                    layer2(t)
                else:
                    layer3(t)

        @block.scalar
        def _(act):
            def prepare_hi(i):
                act.wait_ge(ids_spread_in[i], 16)
                if i >= 2:
                    act.wait_ge(chosen_done, (i - 1) * LOOKUP_CHUNKS)
                nc.scalar.activation(ids_half[0:LOOKUP_P, i % 2, :], ids_spread[0:LOOKUP_P, i, :],
                                     ACT.Copy).then_inc(ids_halved, 1)
                act.wait_ge(table_in[i % 2], 32 * (i // 2 + 1))
                if i >= BUFFERS:
                    act.wait_ge(looked_up, i - BUFFERS + 1)
                nc.scalar.activation(table_parts[0:LOOKUP_P, i % BUFFERS, 0, :], table_sb[0:LOOKUP_P, i % 2, :],
                                     ACT.Copy).then_inc(hi_done, 1)

            def prepare_mid(i):
                act.wait_ge(rest_done, i + 1)
                nc.scalar.activation(table_parts[0:LOOKUP_P, i % BUFFERS, 1, :], table_rest[0:LOOKUP_P, :],
                                     ACT.Copy).then_inc(mid_done, 1)

            def prepare(i):
                prepare_hi(i)
                prepare_mid(i)

            prepare(0)
            prepare(1)
            for what, t, g in STEPS:
                if what == "lookup":
                    if t + 2 < EARLY_LOOKUPS:
                        prepare(t + 2)
                    act.wait_ge(looked_up, t + 1)
                    samples = EARLY_SAMPLES[t]
                    nc.scalar.activation(features[:, samples, ONE_HOT[t] + 1], lookup_ps[t % 2][:, samples],
                                         ACT.Copy).then_inc(lookup_copied, 1)
                elif what == "hi":
                    prepare_hi(t)
                elif what == "mid":
                    prepare_mid(t)
                elif what == "late" and g == PARTS - 1:
                    act.wait_ge(looked_up_late, t - WHOLE_LOOKUPS + 1)
                    nc.scalar.activation(features[:, LATE_SAMPLES, ONE_HOT[t] + 1], late_ps,
                                         ACT.Copy).then_inc(late_copied, 1)
                elif what == "turn" and TURN[t, g] % 2 == 0:
                    act.wait_ge(turned, TURN[t, g] + 1)
                    out, here = copy_of_turned(t, g)
                    nc.scalar.activation(out, here, ACT.Copy).then_inc(features_act, 1)
                elif what == "gram":
                    if t >= 2:
                        act.wait_ge(pairs_turned, t - 1)
                    for piece, (_, runs) in enumerate(PIECES):
                        for run in runs:
                            act.wait_ge(products_done, len(PIECES) * t + piece + 1)
                            out, part = kept_run(t, run)
                            last = nc.scalar.activation(out, part, ACT.Copy)
                    last.then_inc(kept_act, 1)
                elif what == "pairs":
                    own, tile = SPANS[t].partitions, SPANS[t].tile
                    act.wait_ge(pairs_turned, t + 1)
                    if tile >= 2:
                        act.wait_ge(h1_done, 2 * (tile - 1))
                    for k in range(PAIR_BLOCKS):
                        nc.scalar.activation(pairs[:, tile % 2, k, own], pairs_ps[:, k, own],
                                             ACT.Copy).then_inc(pairs_copied, 1)
                elif what == "layer1":
                    if t == 0:
                        act.wait_ge(w_rest_in, 64)
                    else:
                        act.wait_ge(h2_done, t)
                    act.wait_ge(h1_done, 2 * t + 1)
                    for c in range(H1_HALF):
                        nc.scalar.activation(h1[:, c, :], h1_ps[0][:, c, :], ACT.Relu,
                                             bias=b1_sb[:, c:c + 1]).then_inc(h1_relu_act, 1)
                elif what == "layer2":
                    if t >= 1:
                        act.wait_ge(y_done, t)
                    act.wait_ge(h2_done, t + 1)
                    nc.scalar.activation(h2[:, 0, :], h2_ps[0], ACT.Relu, bias=b2_sb[:, 0:1]).then_inc(h2_relu_act, 1)
                elif what == "layer3":
                    act.wait_ge(y_done, t + 1)
                    nc.scalar.activation(y_sb[:, t:t + 1], y_ps, ACT.Copy).then_inc(y_copied, 1)

        @block.vector
        def _(dve):
            def choose(i, chunks):
                dve.wait_ge(ids_halved, i + 1)
                if i == 0:
                    dve.wait_ge(constants_in, 16)
                samples = slice(0, batch) if i < EARLY_LOOKUPS else LATE_SAMPLES
                if i >= BUFFERS:
                    dve.wait_ge(looked_up, i - BUFFERS + 1)
                for c in chunks:
                    nc.vector.tensor_scalar(chosen[0:LOOKUP_P, i % BUFFERS, c, samples],
                                            ids_half[0:LOOKUP_P, i % 2, samples],
                                            row_numbers[0:LOOKUP_P, c:c + 1], None,
                                            ALU.is_equal).then_inc(chosen_done, 1)

            def leave_rest(i):
                dve.wait_ge(hi_done, i + 1)
                if i >= 1:
                    dve.wait_ge(lo_done, i)
                nc.vector.tensor_tensor(table_rest[0:LOOKUP_P, :], table_sb[0:LOOKUP_P, i % 2, :],
                                        table_parts[0:LOOKUP_P, i % BUFFERS, 0, :],
                                        ALU.subtract).then_inc(rest_done, 1)

            def prepare(i):
                early = LOOKUP_CHUNKS // 2 if i == 0 else 0
                if early:
                    choose(i, range(early))
                leave_rest(i)
                choose(i, range(early, LOOKUP_CHUNKS))
                leave_lo(i)

            def leave_lo(i):
                dve.wait_ge(mid_done, i + 1)
                nc.vector.tensor_tensor(table_parts[0:LOOKUP_P, i % BUFFERS, 2, :], table_rest[0:LOOKUP_P, :],
                                        table_parts[0:LOOKUP_P, i % BUFFERS, 1, :], ALU.subtract).then_inc(lo_done, 1)

            nc.vector.memset(zeros[:, :], 0.0).then_inc(zeros_set, 1)
            dve.wait_ge(ids_in, 16)
            nc.vector.tensor_tensor(row_at[:, :], ids_sb[:, 0, :], ids_sb[:, 1, :], ALU.add).then_inc(row_at_done, 1)
            prepare(0)
            prepare(1)
            for what, t, g in STEPS:
                if what == "lookup":
                    if t + 2 < EARLY_LOOKUPS:
                        prepare(t + 2)
                    elif t + 2 == EARLY_LOOKUPS:
                        dve.wait_ge(w1_in, 32)
                        nc.vector.tensor_tensor(w_dense_sum[:, :], w_dense_sb[:, 0, :], w_dense_sb[:, 1, :],
                                                ALU.add).then_inc(w_dense_summed, 1)
                elif what == "hi":
                    choose(t, range(LOOKUP_CHUNKS))
                elif what == "mid":
                    leave_rest(t)
                elif what == "lo":
                    leave_lo(t)
                elif what == "turn" and TURN[t, g] % 2 == 1:
                    dve.wait_ge(turned, TURN[t, g] + 1)
                    out, here = copy_of_turned(t, g)
                    nc.vector.tensor_copy(out, here).then_inc(features_dve, 1)
                elif what == "gram":
                    dve.wait_ge(gram_done, t + 1)
                    if t >= 1:
                        dve.wait_ge(kept_act, t)
                        dve.wait_ge(kept_dve, t)
                    own = SPANS[t].partitions
                    for cols, _ in PIECES:
                        nc.vector.transpose(products[own, cols, :],
                                            gram[own, :, cols].rearrange("p s m -> p m s")).then_inc(products_done, 1)
                    dve.wait_ge(products_done, len(PIECES) * (t + 1))
                    if t >= 2:
                        dve.wait_ge(pairs_turned, t - 1)
                    for run in range(KEPT_BY_VECTOR):
                        out, part = kept_run(t, run)
                        last = nc.vector.tensor_copy(out, part)
                    last.then_inc(kept_dve, 1)
                elif what == "layer1":
                    if t == 0:
                        dve.wait_ge(w_rest_in, 64)
                    else:
                        dve.wait_ge(h2_done, t)
                    dve.wait_ge(h1_done, 2 * t + 2)
                    for c in range(H1_HALF, UNITS1):
                        nc.vector.tensor_scalar(h1[:, c, :], h1_ps[1][:, c - H1_HALF, :], b1_sb[:, c:c + 1],
                                                0.0, ALU.add, ALU.max).then_inc(h1_relu_dve, 1)
                elif what == "layer2":
                    if t >= 1:
                        dve.wait_ge(y_done, t)
                    dve.wait_ge(h2_done, t + 1)
                    nc.vector.tensor_scalar(h2[:, 1, :], h2_ps[1], b2_sb[:, 1:2], 0.0, ALU.add,
                                            ALU.max).then_inc(h2_relu_dve, 1)


def pairs_weights(w_top1, first_pair):
    out = np.zeros((PAIR_BLOCKS * P, w_top1.shape[1]), w_top1.dtype)
    at = 0
    for start, stop, width in KEPT:
        for m in range(start, stop):
            for n in range(width):
                if n <= m:
                    out[at] = w_top1[first_pair + n * SLOTS - n * (n + 1) // 2 + m - n]
                at += 1
    return out.reshape(PAIR_BLOCKS, P, -1).transpose(1, 0, 2)


def kernel(**inputs):
    import concourse.bacc as bacc
    from concourse.bass_utils import run_bass_kernel_spmd

    a = {name: np.asarray(value) for name, value in inputs.items()}
    batch, dim = a["r_dense_features"].shape
    w1 = a["W_top1"]
    n_pairs = SLOTS * (SLOTS - 1) // 2

    def units_on_partitions(w):
        return w.reshape(w.shape[0] // P, P, -1).transpose(1, 0, 2)

    spans = spans_of(batch)
    bases = np.cumsum([0] + [a[f"tbl_{f}"].shape[0] for f in range(TABLES)])
    gathers = list(gathers_of(spans))
    ids_and_bases = np.zeros((P, 2, len(gathers)), np.int32)
    for i, (_, _, samples, slots) in enumerate(gathers):
        size = samples.stop - samples.start
        for k, slot in enumerate(slots):
            here = slice(k * size, (k + 1) * size)
            ids_and_bases[here, 0, i] = a["ids"][samples, slot - 1]
            ids_and_bases[here, 1, i] = bases[slot - 1]

    laid = {
        "dense": a["r_dense_features"],
        "ids_and_bases": ids_and_bases,
        "ids_by_table": a["ids"][:, ONE_HOT].T,
        "constants": np.concatenate([np.eye(P), np.arange(P * LOOKUP_CHUNKS).reshape(P, LOOKUP_CHUNKS)],
                                    axis=1).astype(np.float32),
        "tables": np.concatenate([a[f"tbl_{f}"] for f in range(TABLES)]),
        "w_pairs": pairs_weights(w1, dim),
        "w_dense": np.stack([w1[:dim], w1[dim + n_pairs:]], axis=1),
        "b1": a["b_top1"].reshape(-1, P).T,
        "w2": units_on_partitions(a["W_top2"]),
        "b2": a["b_top2"].reshape(-1, P).T,
        "w3": units_on_partitions(a["W_top3"])[:, :, 0],
    }
    laid = {name: np.ascontiguousarray(value) for name, value in laid.items()}

    nc = bacc.Bacc("TRN2", target_bir_lowering=False, num_devices=1)
    d = {name: nc.dram_tensor(name, v.shape, mybir.dt.from_np(v.dtype), kind="ExternalInput").ap()
         for name, v in laid.items()}
    y = nc.dram_tensor("y", [P, batch // P], F32, kind="ExternalOutput").ap()
    assert all(a[f"tbl_{f}"].shape[0] == LOOKUP_P * LOOKUP_CHUNKS for f in ONE_HOT)
    dlrm_tower(nc, d["dense"], d["ids_and_bases"], d["ids_by_table"], d["constants"],
               d["tables"], [int(bases[f]) for f in ONE_HOT],
               d["w_pairs"], d["w_dense"], d["b1"], d["w2"], d["b2"], d["w3"], y)
    result = run_bass_kernel_spmd(nc, [laid], core_ids=[0])
    return result.results[0]["y"].T.reshape(batch, 1)
```
